# Optimizing a Trainium2 kernel written in Bass

```python
import numpy as np
import jax
import jax.numpy as jnp

def _softmax(x, axis=-1):
    return jax.nn.softmax(x, axis=axis)

def _gelu(x):
    return jax.nn.gelu(x, approximate=True)

def _silu(x):
    return jax.nn.silu(x)

def _sigmoid(x):
    return jax.nn.sigmoid(x)

def _layernorm(x, axis=-1, eps=1e-05):
    m = jnp.mean(x, axis=axis, keepdims=True)
    v = jnp.var(x, axis=axis, keepdims=True)
    return (x - m) / jnp.sqrt(v + eps)

def _scatter_add(tgt, idx, src, axis=0):
    return tgt.at[idx].add(src)

def _segment_sum(src, seg, n):
    return jax.ops.segment_sum(src, seg, n)
kernel_name = 'mk_xattn_ffn_d1_seqx_r4_ac5f2b'

def setup_inputs(seed: int=0):
    np.random.seed(seed)
    _w = jnp.asarray

    def _rec_inputs():
        import jax
        import jax.numpy as jnp
        _rk = jax.random.key(seed)
        x = -0.0002928 + 1 * jax.random.normal(jax.random.fold_in(_rk, 1), (128, 128, 256), jnp.float32)
        _lenS = 128 - jax.random.randint(jax.random.fold_in(_rk, 7), (128,), 0, max(1, 128 // 4) + 1, jnp.int32)
        _lenS2 = 128 - jax.random.randint(jax.random.fold_in(_rk, 8), (128,), 0, max(1, 128 // 4) + 1, jnp.int32)
        _ctx_1024P = jax.random.normal(jax.random.fold_in(_rk, 11), (128, 16, 256), jnp.float32)
        _ctx_1024c = jax.random.dirichlet(jax.random.fold_in(_rk, 511), 0.3 * jnp.ones((16,), jnp.float32), (128, 128))
        _ctx_1024t = jnp.einsum('bsk,bkd->bsd', _ctx_1024c, _ctx_1024P)
        _ctx_1024t = _ctx_1024t * jax.lax.rsqrt(jnp.mean(jnp.square(_ctx_1024t)) + 1e-12) * 0.953939
        ctx_1024 = -1.39393e-06 + 0.999914 * (_ctx_1024t + 0.3 * jax.random.normal(jax.random.fold_in(_rk, 611), (128, 128, 256), jnp.float32))
        return (x, ctx_1024)
    x, ctx_1024 = _rec_inputs()

    def _L0_xattn_setup():
        import jax, jax.numpy as jnp
        import numpy as np
        import math
        B, T, E, H = (2, 512, 256, 16)
        D = E // H
        key = jax.random.key(seed)
        ks = jax.random.split(key, 8)
        s = 1.0 / math.sqrt(E)
        return {'input': jax.random.normal(ks[0], (B, T, E), jnp.float32), 'encoded_features': jax.random.normal(ks[1], (B, T, E), jnp.float32), 'Wq': jax.random.normal(ks[2], (E, E), jnp.float32) * s, 'bq': jnp.zeros((E,), jnp.float32), 'Wkv': jax.random.normal(ks[3], (E, 2 * E), jnp.float32) * s, 'bkv': jnp.zeros((2 * E,), jnp.float32), 'Wo': jax.random.normal(ks[4], (E, E), jnp.float32) * s, 'bo': jnp.zeros((E,), jnp.float32)}
    _L0_xattn_all = _L0_xattn_setup()
    _L0_xattn_in = {k: v for k, v in _L0_xattn_all.items() if k in ('Wq', 'bq', 'Wkv', 'bkv', 'Wo', 'bo')}
    del _L0_xattn_all

    def _L0_ffn_setup():
        import jax, jax.numpy as jnp
        import numpy as np
        CAPACITY_RATIO = 0.75
        key = jax.random.key(seed)
        k1, k2, k3 = jax.random.split(key, 3)
        B, L, D = (4, 2048, 256)
        x = jax.random.normal(k1, (B, L, D), dtype=jnp.float32)
        w_router = jax.random.normal(k2, (D,), dtype=jnp.float32) * 0.02
        w_block = jax.random.normal(k3, (D, D), dtype=jnp.float32) * 0.02
        return {'x': x, 'w_router': w_router, 'w_block': w_block}
    _L0_ffn_all = _L0_ffn_setup()
    _L0_ffn_in = {k: v for k, v in _L0_ffn_all.items() if k in ('w_router', 'w_block')}
    del _L0_ffn_all
    return {'x': x, 'ctx_1024': ctx_1024, 'L0_xattn_Wq': _L0_xattn_in['Wq'], 'L0_xattn_bq': _L0_xattn_in['bq'], 'L0_xattn_Wkv': _L0_xattn_in['Wkv'], 'L0_xattn_bkv': _L0_xattn_in['bkv'], 'L0_xattn_Wo': _L0_xattn_in['Wo'], 'L0_xattn_bo': _L0_xattn_in['bo'], 'L0_ffn_w_router': _L0_ffn_in['w_router'], 'L0_ffn_w_block': _L0_ffn_in['w_block']}

def reference(x, ctx_1024, L0_xattn_Wq, L0_xattn_bq, L0_xattn_Wkv, L0_xattn_bkv, L0_xattn_Wo, L0_xattn_bo, L0_ffn_w_router, L0_ffn_w_block):
    import jax
    import jax.numpy as jnp

    def _L0_xattn_ref(input, encoded_features, Wq, bq, Wkv, bkv, Wo, bo):
        import jax, jax.numpy as jnp
        import numpy as np
        import math
        B, T, E, H = (2, 512, 256, 16)
        D = E // H
        b, tq, _ = input.shape
        tk = encoded_features.shape[1]
        q = (input @ Wq + bq).reshape(b, tq, H, D).transpose(0, 2, 1, 3)
        kv = (encoded_features @ Wkv + bkv).reshape(b, tk, 2, H, D).transpose(2, 0, 3, 1, 4)
        k, v = (kv[0], kv[1])
        scores = jnp.einsum('bhqd,bhkd->bhqk', q, k) / math.sqrt(D)
        attn = jax.nn.softmax(scores, axis=2)
        out = jnp.einsum('bhqk,bhkd->bhqd', attn, v)
        out = out.transpose(0, 2, 1, 3).reshape(b, tq, H * D)
        return out @ Wo + bo

    def _L0_ffn_ref(x, w_router, w_block):
        import jax, jax.numpy as jnp
        import numpy as np
        CAPACITY_RATIO = 0.75
        B, L, D = x.shape
        k = max(1, int(L * CAPACITY_RATIO))
        scores = jnp.einsum('bld,d->bl', x, w_router)
        _, top_idx = jax.lax.top_k(scores, k)
        selected = jnp.take_along_axis(x, top_idx[:, :, None], axis=1)
        processed = jax.nn.gelu(jnp.einsum('bkd,de->bke', selected, w_block))
        batch_idx = jnp.arange(B)[:, None]
        out = x.at[batch_idx, top_idx].set(processed)
        return out
    x = x + _L0_xattn_ref(_layernorm(x, axis=-1), ctx_1024, L0_xattn_Wq, L0_xattn_bq, L0_xattn_Wkv, L0_xattn_bkv, L0_xattn_Wo, L0_xattn_bo)
    x = x + _L0_ffn_ref(_layernorm(x, axis=-1), L0_ffn_w_router, L0_ffn_w_block)
    return x

_drawn_inputs = setup_inputs


def setup_inputs(seed=0):
    import zlib

    import numpy as np

    out = dict(_drawn_inputs(seed))
    spreads = {'L0_xattn_bq': (0.0, 0.1), 'L0_xattn_bkv': (0.0, 0.1), 'L0_xattn_bo': (0.0, 0.1)}
    factors = {}
    for name, (base, spread) in spreads.items():
        noise = np.random.default_rng([zlib.crc32(name.encode()), seed]).standard_normal(out[name].shape)
        drawn = base * np.exp(spread * noise) if base else spread * noise
        out[name] = jnp.asarray(drawn.astype(out[name].dtype))
    for name, factor in factors.items():
        out[name] = (out[name] * factor).astype(out[name].dtype)
    return out
```

```python
from contextlib import ExitStack

import concourse.bass as bass
from concourse import mybir


def cross_attention_routed_ffn(
    nc: bass.Bass,
    x: bass.AP,
    ctx_in: bass.AP,
    w_q: bass.AP,
    b_q: bass.AP,
    w_kv: bass.AP,
    b_kv: bass.AP,
    w_o: bass.AP,
    b_o: bass.AP,
    w_router: bass.AP,
    w_block: bass.AP,
    out: bass.AP,
):
    f32 = mybir.dt.float32
    f32r = mybir.dt.float32r
    ALU = mybir.AluOpType
    ACT = mybir.ActivationFunctionType
    AX = mybir.AxisListType

    B, T, E = x.shape
    H = 16
    D = E // H
    P = 128
    C = E // P
    J = 4
    KEEP = int(T * 0.75)
    DROP = T - KEEP
    EPS = 1e-5
    LOWEST = -3.4028234663852886e38
    SCALE = 1.0 / D ** 0.5
    assert T == P and E == C * P and B % 16 == 0 and DROP % 8 == 0

    BODY = 16
    GROUP = 8
    ZW = E + 2

    ctx = ExitStack()
    with ctx:
        def sb(name, shape, dt=f32):
            return ctx.enter_context(nc.sbuf_tensor(name, shape, dt))

        def sem(name):
            return ctx.enter_context(nc.semaphore(name))

        x_sb = sb("x_sb", [P, 8, E])
        c_sb = sb("c_sb", [P, 8, E])
        xb_sb = sb("xb_sb", [P, 8, E])
        xhat = sb("xhat", [P, 2, E])
        t_hi = sb("t_hi", [P, 4, 2, C, 2 * T], f32r)
        t_lo = sb("t_lo", [P, 4, 2, C, 2 * T], f32r)
        q_raw = sb("q_raw", [P, C, 2, T])
        q_eo = sb("q_eo", [P, 2, C, 2, 2, T])
        k_sb = sb("k_sb", [P, 2, C, 2 * T])
        v_sb = sb("v_sb", [P, 2, E])
        v_pad = sb("v_pad", [P, 2, H // 2, 2, 2 * D])
        e_sb = sb("e_sb", [P, 2, J, C, 2, T])
        o_hi = sb("o_hi", [P, 2, E], f32r)
        o_lo = sb("o_lo", [P, 2, E], f32r)
        x1_sb = sb("x1_sb", [P, 4, E])
        y_sb = sb("y_sb", [P, 16, E])
        y_hi = sb("y_hi", [P, 2, E], f32r)
        y_lo = sb("y_lo", [P, 2, E], f32r)
        z_sb = sb("z_sb", [P, 16, ZW])
        s_sb = sb("s_sb", [P, 16, E])
        w_hi = {n: sb(f"w_{n}_hi", [P, C, ZW if n == "z" else E], f32r) for n in "qkvoz"}
        w_lo = {n: sb(f"w_{n}_lo", [P, C, ZW if n == "z" else E], f32r) for n in "qkvoz"}
        bq_sb = sb("bq_sb", [P, C])
        bk_sb = sb("bk_sb", [P, C])
        bv_sb = sb("bv_sb", [P, E])
        bo_sb = sb("bo_sb", [P, E])
        ident = sb("ident", [P, P])
        head_mask = sb("head_mask", [P, 2])
        eps_sb = sb("eps_sb", [P, 1])
        minus_half = sb("minus_half", [P, 1])
        st1 = sb("st1", [P, 2, 6])
        mv1 = sb("mv1", [P, 4, 2])
        ve1 = sb("ve1", [P, 4])
        rstd1 = sb("rstd1", [P, 4])
        st2 = sb("st2", [P, 2, 6])
        mv2 = sb("mv2", [P, 4, 2])
        ve2 = sb("ve2", [P, 4])
        rstd2 = sb("rstd2", [P, 4])
        neg_max = sb("neg_max", [P, 2, H])
        sums = sb("sums", [P, 2, H])
        recip = sb("recip", [P, 2, H])
        fence_sb = sb("fence_sb", [1, 1])
        cand = sb("cand", [GROUP, T])
        top8 = sb("top8", [GROUP, 8])
        keep_row = sb("keep_row", [GROUP, T])
        keep_col = sb("keep_col", [P, 2, GROUP])

        raw = e_sb[:, :, :, :, :, :].rearrange("p a b c d e -> p (a b c d e)")
        raw_w, at = {}, 0
        for n in "qkvoz":
            width = ZW if n == "z" else E
            raw_w[n] = raw[:, at:at + C * width].rearrange("p (c e) -> p c e", c=C)
            at += C * width

        ps_s = ctx.enter_context(nc.psum_tensor("ps_s", [P, J, C, 2, T], f32))
        ps_a = ctx.enter_context(nc.psum_tensor("ps_a", [P, 512], f32))
        ps_y = ctx.enter_context(nc.psum_tensor("ps_y", [P, 512], f32))
        ps_t = ctx.enter_context(nc.psum_tensor("ps_t", [P, 512], f32))
        ps_q = ctx.enter_context(nc.psum_tensor("ps_q", [P, 512], f32))

        x_in = [sem(f"x_in{i}") for i in range(8)]
        c_in = [sem(f"c_in{i}") for i in range(8)]
        stored = [sem(f"stored{i}") for i in range(4)]
        w_in = sem("w_in")
        const_ready = sem("const_ready")
        mask_step = sem("mask_step")
        v_pad_zero = sem("v_pad_zero")
        parity_ready = sem("parity_ready")
        head_mask_ready = sem("head_mask_ready")
        w_hi_ready = sem("w_hi_ready")
        w_lo_ready = sem("w_lo_ready")
        st1_ready, mv1_ready, ve1_ready, rstd1_ready = sem("st1_r"), sem("mv1_r"), sem("ve1_r"), sem("rstd1_r")
        st2_ready, mv2_ready, ve2_ready, rstd2_ready = sem("st2_r"), sem("mv2_r"), sem("ve2_r"), sem("rstd2_r")
        xhat_ready = sem("xhat_ready")
        xb_ready = sem("xb_ready")
        t_mm = sem("t_mm")
        t_hi_ready = sem("t_hi_ready")
        t_lo_ready = sem("t_lo_ready")
        q_mm = sem("q_mm")
        q_raw_ready = sem("q_raw_ready")
        q_eo_ready = sem("q_eo_ready")
        k_mm = sem("k_mm")
        k_ready = sem("k_ready")
        s_mm = [sem(f"s_mm{j}") for j in range(J)]
        max_ready = [sem(f"max_ready{j}") for j in range(3)]
        exp_ready = [sem(f"exp_ready{j}") for j in range(J)]
        sum01_ready = sem("sum01_ready")
        recip_ready = sem("recip_ready")
        v_mm = sem("v_mm")
        v_ready = sem("v_ready")
        v_pad_ready = sem("v_pad_ready")
        a_mm = sem("a_mm")
        o_hi_ready = sem("o_hi_ready")
        o_lo_ready = sem("o_lo_ready")
        o_mm = sem("o_mm")
        x1_ready = sem("x1_ready")
        y_ready = sem("y_ready")
        y_mm = sem("y_mm")
        y_hi_ready = sem("y_hi_ready")
        y_lo_ready = sem("y_lo_ready")
        z_mm = sem("z_mm")
        z_ready = sem("z_ready")
        s_ready = sem("s_ready")
        gelu_ready = sem("gelu_ready")
        d_ready = sem("d_ready")
        score_mm = sem("score_mm")
        cand_ready = sem("cand_ready")
        top_found = sem("top_found")
        top_dropped = sem("top_dropped")
        keep_row_ready = sem("keep_row_ready")
        keep_mm = sem("keep_mm")
        keep_col_ready = sem("keep_col_ready")
        final_ready = sem("final_ready")

        block = ctx.enter_context(nc.Block())

        class Slot:

            def __init__(self, eng, i, u, values):
                self.eng, self.i, self.u, self.values = eng, i, u, values

            def has(self, lag, count=1):
                if not isinstance(self.i, int):
                    return True
                b = BODY * self.i + self.u + lag
                return 0 <= b and b + count <= B

            def rows(self, dram, lag, count):
                b = self.u + lag
                view = dram.rearrange("(n b) t e -> n t b e", b=BODY)
                return view[self.i + b // BODY, :, b % BODY:b % BODY + count, :]

            def wait(self, semaphore, lag):
                k = self.u + lag + 1
                self.wait_value(semaphore, k)

            def wait_value(self, semaphore, k):
                if isinstance(self.i, int):
                    if BODY * self.i + k > 0:
                        self.eng.wait_ge(semaphore, min(BODY * self.i + k, B))
                    return
                assert BODY + k > 0
                if k not in self.values:
                    self.values[k] = self.eng.snap(self.i * BODY + k)
                self.eng.wait_ge(semaphore, self.values[k])

            def wait_dma(self, sems, lag, per):
                b = self.u + lag
                semaphore = sems[(b // per) % len(sems)]
                self.wait_value(semaphore, 16 * (b // 16) + 16)

        def run(eng, slot, first, last):
            n = B // BODY
            for u in range(first, BODY):
                slot(Slot(eng, 0, u, {}))
            with eng.Fori(1, n - 1) as i:
                values = {}
                for u in range(BODY):
                    slot(Slot(eng, i, u, values))
            for u in range(last - (n - 1) * BODY):
                slot(Slot(eng, n - 1, u, {}))

        def group_at(s, phase, lag):
            return s.u % GROUP == phase and s.has(-lag, GROUP)

        FIRST, LAST = -6, B + 10

        @block.sync
        def _(sp):
            for n, src in (("q", w_q), ("k", w_kv[:, 0:E]), ("v", w_kv[:, E:2 * E]), ("o", w_o)):
                sp.dma_start(raw_w[n], src.rearrange("(c p) e -> p c e", p=P)).then_inc(w_in, 16)
            sp.dma_start(raw_w["z"][:, :, 0:E], w_block.rearrange("(c p) e -> p c e", p=P)).then_inc(w_in, 16)
            with nc.allow_non_contiguous_dma(reason="vectors of 256 elements, once"):
                sp.dma_start(raw_w["z"][:, :, E:E + 1], w_router.rearrange("(c p a) -> p c a", p=P, a=1)).then_inc(w_in, 16)
                sp.dma_start(bq_sb[:, :], b_q.rearrange("(c p) -> p c", p=P)).then_inc(w_in, 16)
                sp.dma_start(bk_sb[:, :], b_kv[0:E].rearrange("(c p) -> p c", p=P)).then_inc(w_in, 16)
            sp.dma_start(bv_sb[:, :], b_kv[E:2 * E].rearrange("(a e) -> a e", a=1).to_broadcast([P, E])).then_inc(w_in, 16)
            sp.dma_start(bo_sb[:, :], b_o.rearrange("(a e) -> a e", a=1).to_broadcast([P, E])).then_inc(w_in, 16)

            def slot(s):
                if s.u % 2 == 0 and s.has(10):
                    s.wait(xhat_ready, 3)
                    s.wait(xb_ready, 3)
                    s.wait(t_mm, 3)
                    r = (s.u + 10) % 8
                    n = ((s.u + 10) // 2) % 8
                    sp.dma_start(x_sb[:, r:r + 2, :], s.rows(x, 10, 2)).then_inc(x_in[n], 16)
                    sp.dma_start(c_sb[:, r:r + 2, :], s.rows(ctx_in, 10, 2)).then_inc(c_in[n], 16)
                for phase, lag in ((0, 16), (2, 14)):
                    if s.u % GROUP == phase and s.has(-lag, 4):
                        s.wait(final_ready, 3 - lag)
                        r = (s.u - lag) % 16
                        sp.dma_start(s.rows(out, -lag, 4),
                                     s_sb[:, r:r + 4, :]).then_inc(stored[(r // 4) % 4], 16)

            run(sp, slot, -10, LAST + 3)
            for n in range(4):
                sp.wait_ge(stored[n], B)

        @block.tensor
        def _(pe):
            pe.wait_ge(const_ready, 1)
            pe.wait_ge(w_hi_ready, 1)
            pe.wait_ge(w_lo_ready, 1)

            def three_terms(dst, lhs, rhs):
                terms = [(a, b) for a, b in ((0, 0), (1, 0), (0, 1))]
                for c in range(C):
                    for n, (a, b) in enumerate(terms):
                        last = nc.tensor.matmul(dst, lhs(a, c), rhs(b, c), start=(c == 0 and n == 0),
                                                stop=(c == C - 1 and n == len(terms) - 1))
                return last

            def slot(s):
                u = s.u
                if s.has(0):
                    r2, h = (u // 2) % 2, u % 2
                    if u % 2 == 0:
                        s.wait(q_eo_ready, 1)
                        s.wait(k_ready, 1)
                    for c in range(C):
                        for j in range(J):
                            if c == 0:
                                s.wait(exp_ready[j], -1)
                            rows = slice(32 * j, 32 * j + 32)
                            mm = nc.tensor.matmul(ps_s[:, j, c, :, :], k_sb[rows, r2, c, h * T:(h + 1) * T],
                                                  q_eo[rows, r2, c, h, :, :], start=True, stop=True)
                            if c == C - 1:
                                mm.then_inc(s_mm[j], 1)
                if s.has(-1):
                    r = (u - 1) % 2
                    s.wait(v_pad_ready, -1)
                    s.wait(x1_ready, -2)
                    for c in range(C):
                        for par in range(2):
                            for j in range(J):
                                mm = nc.tensor.matmul(ps_a[32 * j:32 * j + 32, c * T:(c + 1) * T],
                                                      v_pad[:, r, c * J + j, par, :], e_sb[:, r, j, c, par, :],
                                                      start=(par == 0), stop=(par == 1))
                    mm.then_inc(a_mm, 1)
                if s.has(-2):
                    s.wait(y_ready, -2)
                    s.wait(v_ready, -1)
                    for c in range(C):
                        mm = nc.tensor.transpose(ps_y[:, c * T:(c + 1) * T], y_sb[:, (u - 2) % 16, c * P:(c + 1) * P], ident[:, :])
                    mm.then_inc(y_mm, 1)
                if s.has(4):
                    s.wait(xhat_ready, 4)
                    if u % 2 == 0:
                        s.wait_dma(c_in, 4, 2)
                    s.wait(z_ready, -3)
                    for kind in range(2):
                        for c in range(C):
                            src = (xhat[:, (u + 4) % 2, c * P:(c + 1) * P] if kind == 0
                                   else c_sb[:, (u + 4) % 8, c * P:(c + 1) * P])
                            n = kind * C + c
                            mm = nc.tensor.transpose(ps_t[:, n * T:(n + 1) * T], src, ident[:, :])
                    mm.then_inc(t_mm, 1)
                kind, lag = (0, 2) if u % 2 == 0 else (1, 1)
                if s.has(lag):
                    pair = ((u + lag) // 2) % 4
                    if kind == 0:
                        s.wait(t_lo_ready, 3)
                        s.wait(k_ready, 1)
                        if group_at(s, 6, 14):
                            s.wait(keep_col_ready, -7)
                    else:
                        s.wait(q_raw_ready, 2)
                        if group_at(s, 3, 11):
                            s.wait(cand_ready, -4)
                    w = "qk"[kind]
                    for m in range(C):
                        mm = three_terms(ps_q[:, m * 2 * T:(m + 1) * 2 * T],
                                         lambda a, c: (w_hi, w_lo)[a][w][:, c, m * P:(m + 1) * P],
                                         lambda a, c: (t_hi, t_lo)[a][:, pair, kind, c, :])
                    mm.then_inc((q_mm, k_mm)[kind], 2)
                if s.has(0):
                    s.wait(y_lo_ready, -2)
                    pair, h = (u // 2) % 4, u % 2
                    three_terms(ps_y[:, 0:E],
                                lambda a, c: (t_hi, t_lo)[a][:, pair, 1, c, h * T:(h + 1) * T],
                                lambda a, c: (w_hi, w_lo)[a]["v"][:, c, :]).then_inc(v_mm, 1)
                if s.has(-1):
                    s.wait(o_lo_ready, -1)
                    three_terms(ps_a[:, 0:E],
                                lambda a, c: (o_hi, o_lo)[a][:, (u - 1) % 2, c * T:(c + 1) * T],
                                lambda a, c: (w_hi, w_lo)[a]["o"][:, c, :]).then_inc(o_mm, 1)
                if s.has(-2):
                    s.wait(y_lo_ready, -2)
                    s.wait(t_lo_ready, 4)
                    three_terms(ps_t[:, 0:ZW],
                                lambda a, c: (y_hi, y_lo)[a][:, (u - 2) % 2, c * T:(c + 1) * T],
                                lambda a, c: (w_hi, w_lo)[a]["z"][:, c, :]).then_inc(z_mm, 1)
                if group_at(s, 2, 10):
                    s.wait(z_ready, -3)
                    s.wait(q_raw_ready, 3)
                    s.wait(keep_col_ready, -11)
                    r = (u - 10) % 16
                    nc.tensor.transpose(ps_q[0:GROUP, 0:T], z_sb[:, r:r + GROUP, E], ident[:, :]).then_inc(score_mm, 8)
                if group_at(s, 5, 13):
                    s.wait(keep_row_ready, -6)
                    s.wait(k_ready, 2)
                    nc.tensor.transpose(ps_q[:, 0:GROUP], keep_row[:, :], ident[0:GROUP, 0:GROUP]).then_inc(keep_mm, 8)

            run(pe, slot, FIRST, LAST)

        @block.scalar
        def _(act):
            act.wait_ge(w_in, 160)
            act.wait_ge(const_ready, 1)
            for n in "qkvoz":
                last = nc.scalar.copy(w_hi[n][:, :, :], raw_w[n])
            last.then_inc(w_hi_ready, 1)
            act.wait_ge(w_lo_ready, 1)

            def exps(s, j):
                r = s.u % 2
                s.wait(max_ready[min(j, 2)], 0)
                if j == 0:
                    s.wait(a_mm, -2)
                for c in range(C):
                    for par in range(2):
                        h = c * 2 * J + 2 * j + par
                        extra = {} if j < 2 else {"accum_out": sums[:, r, h:h + 1]}
                        last = nc.scalar.activation(e_sb[:, r, j, c, par, :], ps_s[:, j, c, par, :], ACT.Exp,
                                                    bias=neg_max[:, r, h:h + 1], **extra)
                last.then_inc(exp_ready[j], 1)

            def slot(s):
                u = s.u
                if s.has(0):
                    exps(s, 0)
                if s.has(-1):
                    s.wait(a_mm, -1)
                    s.wait(o_mm, -3)
                    nc.scalar.copy(o_hi[:, (u - 1) % 2, :], ps_a[:, 0:E]).then_inc(o_hi_ready, 1)
                if s.has(-2):
                    s.wait(y_mm, -2)
                    s.wait(z_mm, -4)
                    nc.scalar.copy(y_hi[:, (u - 2) % 2, :], ps_y[:, 0:E]).then_inc(y_hi_ready, 1)
                if s.has(0):
                    exps(s, 1)
                if s.has(4):
                    s.wait(t_mm, 4)
                    s.wait(v_mm, -4)
                    pair, h = ((u + 4) // 2) % 4, u % 2
                    nc.scalar.copy(t_hi[:, pair, :, :, h * T:(h + 1) * T].rearrange("p k c t -> p (k c) t"),
                                   ps_t[:, :].rearrange("p (n t) -> p n t", t=T)).then_inc(t_hi_ready, 1)
                if s.has(0):
                    exps(s, 2)
                if u % 2 == 1 and s.has(1):
                    s.wait(k_mm, 2)
                    s.wait(s_mm[J - 1], -2)
                    for c in range(C):
                        last = nc.scalar.activation(k_sb[:, ((u + 1) // 2) % 2, c, :], ps_q[:, c * 2 * T:(c + 1) * 2 * T],
                                                    ACT.Identity, bias=bk_sb[:, c:c + 1])
                    last.then_inc(k_ready, 2)
                if s.has(0):
                    exps(s, 3)
                if s.has(-2):
                    s.wait(z_mm, -2)
                    s.wait(final_ready, -16)
                    nc.scalar.copy(z_sb[:, (u - 2) % 16, :], ps_t[:, 0:ZW]).then_inc(z_ready, 1)
                for phase, lag in ((2, 10), (3, 7)):
                    if s.u % GROUP == phase and s.has(-lag, 4):
                        s.wait(z_ready, 3 - lag)
                        r = (u - lag) % 16
                        z = z_sb[:, r:r + 4, 0:E]
                        nc.scalar.activation(z, z, ACT.Gelu_apprx_tanh).then_inc(gelu_ready, 4)

            run(act, slot, FIRST, LAST)

        @block.vector
        def _(dve):
            nc.vector.memset(v_pad[:, :, :, :, :], 0.0).then_inc(v_pad_zero, 1)
            dve.wait_ge(const_ready, 1)
            nc.vector.tensor_reduce(head_mask[:, :], ident[:, :].rearrange("p (g q d) -> p q g d", q=2, d=D), AX.XY,
                                    ALU.add).then_inc(parity_ready, 1)
            dve.wait_ge(parity_ready, 1)
            nc.vector.tensor_scalar(head_mask[:, :], head_mask[:, :], SCALE, None, ALU.mult).then_inc(head_mask_ready, 1)
            dve.wait_ge(w_hi_ready, 1)
            for n in "qkvoz":
                last = nc.vector.tensor_tensor(w_lo[n][:, :, :], raw_w[n], w_hi[n][:, :, :].bitcast(f32), ALU.subtract)
            last.then_inc(w_lo_ready, 1)

            def slot(s):
                u = s.u
                if group_at(s, 3, 11):
                    s.wait(score_mm, -4)
                    nc.vector.tensor_scalar(cand[:, :], ps_q[0:GROUP, 0:T][:, ::-1], -1.0, None, ALU.mult).then_inc(cand_ready, 8)
                if s.has(-1):
                    s.wait(exp_ready[3], -1)
                    s.wait(sum01_ready, -1)
                    nc.vector.reciprocal(recip[:, (u - 1) % 2, :], sums[:, (u - 1) % 2, :]).then_inc(recip_ready, 1)
                if s.has(-2):
                    r = (u - 2) % 4
                    s.wait(rstd2_ready, -2)
                    s.wait(d_ready, -16)
                    nc.vector.tensor_scalar(y_sb[:, (u - 2) % 16, :], x1_sb[:, r, :], mv2[:, r, 0:1], rstd2[:, r:r + 1],
                                            ALU.subtract, ALU.mult).then_inc(y_ready, 1)
                if s.has(6):
                    if u % 2 == 0:
                        s.wait_dma(x_in, 6, 2)
                    nc.vector.bn_stats(st1[:, u % 2, :], x_sb[:, (u + 6) % 8, :]).then_inc(st1_ready, 1)
                if s.has(0):
                    for n, (j0, j1) in enumerate(((0, 1), (1, 2), (2, 4))):
                        s.wait(s_mm[j1 - 1], 0)
                        dst = neg_max[:, u % 2, :].rearrange("p (c j q) -> p j c q", c=C, j=J)[:, j0:j1, :, :]
                        src = ps_s[:, j0:j1, :, :, :]
                        if j1 - j0 == 1:
                            dst, src = dst[:, 0, :, :], src[:, 0, :, :, :]
                        nc.vector.tensor_reduce(dst, src, AX.X, ALU.max, negate=True).then_inc(max_ready[n], 1)
                if s.has(-1):
                    s.wait(o_hi_ready, -1)
                    nc.vector.tensor_tensor(o_lo[:, (u - 1) % 2, :], ps_a[:, 0:E], o_hi[:, (u - 1) % 2, :].bitcast(f32),
                                            ALU.subtract).then_inc(o_lo_ready, 1)
                if s.has(-2):
                    s.wait(y_hi_ready, -2)
                    nc.vector.tensor_tensor(y_lo[:, u % 2, :], ps_y[:, 0:E], y_hi[:, u % 2, :].bitcast(f32),
                                            ALU.subtract).then_inc(y_lo_ready, 1)
                if s.has(4):
                    pair, h = ((u + 4) // 2) % 4, u % 2
                    s.wait(t_hi_ready, 4)
                    part = (slice(None), pair, slice(None), slice(None), slice(h * T, (h + 1) * T))
                    nc.vector.tensor_tensor(t_lo[part].rearrange("p k c t -> p (k c) t"),
                                            ps_t[:, :].rearrange("p (n t) -> p n t", t=T),
                                            t_hi[part].rearrange("p k c t -> p (k c) t").bitcast(f32),
                                            ALU.subtract).then_inc(t_lo_ready, 1)
                if u % 2 == 0 and s.has(2):
                    s.wait(q_mm, 3)
                    s.wait(q_eo_ready, 1)
                    nc.vector.tensor_tensor(q_raw[:, :, :, :].rearrange("p c b t -> p c (b t)"),
                                            ps_q[:, :].rearrange("p (c t) -> p c t", c=C),
                                            bq_sb[:, :].rearrange("p (c a) -> p c a", a=1).to_broadcast([P, C, 2 * T]),
                                            ALU.add).then_inc(q_raw_ready, 2)
                if s.has(0):
                    s.wait(v_mm, 0)
                    s.wait(v_pad_ready, -2)
                    nc.vector.tensor_tensor(v_sb[:, u % 2, :], ps_y[:, 0:E], bv_sb[:, :], ALU.add).then_inc(v_ready, 1)
                    s.wait(exp_ready[1], 0)
                    nc.vector.tensor_reduce(
                        sums[:, u % 2, :].rearrange("p (c j q) -> p j c q", c=C, j=J)[:, 0:2, :, :],
                        e_sb[:, u % 2, 0:2, :, :, :], AX.X, ALU.add).then_inc(sum01_ready, 1)
                if s.has(-1):
                    s.wait(o_mm, -1)
                    s.wait(xb_ready, -1)
                    s.wait(s_ready, -5)
                    r = (u - 1) % 4
                    nc.vector.tensor_tensor(x1_sb[:, r, :], ps_a[:, 0:E], xb_sb[:, (u - 1) % 8, :], ALU.add).then_inc(x1_ready, 1)
                    s.wait(x1_ready, -1)
                    nc.vector.bn_stats(st2[:, (u - 1) % 2, :], x1_sb[:, r, :]).then_inc(st2_ready, 1)
                if s.has(5):
                    r = (u + 5) % 4
                    s.wait(rstd1_ready, 5)
                    s.wait(t_mm, 3)
                    if s.has(6):
                        s.wait(st1_ready, 6)
                    if s.has(-1):
                        s.wait(st2_ready, -1)
                    nc.vector.tensor_scalar(xhat[:, (u + 5) % 2, :], x_sb[:, (u + 5) % 8, :], mv1[:, r, 0:1], rstd1[:, r:r + 1],
                                            ALU.subtract, ALU.mult).then_inc(xhat_ready, 1)
                else:
                    if s.has(6):
                        s.wait(st1_ready, 6)
                    if s.has(-1):
                        s.wait(st2_ready, -1)
                if s.has(6):
                    nc.vector.bn_aggr(mv1[:, (u + 6) % 4, :], st1[:, u % 2, :]).then_inc(mv1_ready, 1)
                if s.has(-1):
                    nc.vector.bn_aggr(mv2[:, (u - 1) % 4, :], st2[:, (u - 1) % 2, :]).then_inc(mv2_ready, 1)
                for phase, lag in ((3, 11), (4, 12)):
                    if group_at(s, phase, lag):
                        for n in range(2):
                            rnd = 2 * (phase - 3) + n
                            if rnd == 0:
                                s.wait(cand_ready, 7 - lag)
                            else:
                                s.wait(top_dropped, 2 * rnd - 1 - lag)
                            fence()
                            nc.vector.max(top8[:, :], cand[:, :]).then_inc(top_found, 2)
                            s.wait(top_found, 2 * rnd + 1 - lag)
                            fence()
                            nc.vector.match_replace(cand[:, :], top8[:, :], cand[:, :], LOWEST).then_inc(top_dropped, 2)
                if group_at(s, 4, 12):
                    s.wait(top_dropped, -5)
                    s.wait(keep_mm, -13)
                    nc.vector.tensor_scalar(keep_row[:, ::-1], cand[:, :], LOWEST, None, ALU.is_gt).then_inc(keep_row_ready, 8)
                if group_at(s, 5, 13):
                    s.wait(keep_mm, -6)
                    nc.vector.tensor_copy(keep_col[:, ((u - 13) // 8) % 2, :], ps_q[:, 0:GROUP]).then_inc(keep_col_ready, 8)
                for phase, lag in ((6, 14), (7, 13), (0, 12), (1, 11)):
                    if u % GROUP == phase and s.has(-lag, 2):
                        s.wait(d_ready, 1 - lag)
                        if phase == 6:
                            s.wait(keep_col_ready, 7 - lag)
                        for b in range(2):
                            k = u - lag + b
                            nc.vector.scalar_tensor_tensor(s_sb[:, k % 16, :], z_sb[:, k % 16, 0:E],
                                                           keep_col[:, (k // 8) % 2, k % 8:k % 8 + 1], s_sb[:, k % 16, :],
                                                           ALU.mult, ALU.add).then_inc(final_ready, 1)

            def fence():
                nc.vector.memset(fence_sb[:, :], 0.0)

            run(dve, slot, FIRST, LAST)

        @block.gpsimd
        def _(pool):
            nc.gpsimd.memset(ident[:, :], 0.0).then_inc(mask_step, 1)
            nc.gpsimd.memset(eps_sb[:, :], EPS).then_inc(mask_step, 1)
            nc.gpsimd.memset(minus_half[:, :], -0.5).then_inc(mask_step, 1)
            nc.gpsimd.memset(raw_w["z"][:, :, E + 1:E + 2], 0.0).then_inc(mask_step, 1)
            pool.wait_ge(mask_step, 4)
            nc.gpsimd.affine_select(out=ident[:, :], in_=ident[:, :], compare_op=ALU.not_equal, fill=1.0, base=0,
                                    pattern=[[-1, P]], channel_multiplier=1).then_inc(const_ready, 1)
            pool.wait_ge(w_in, 160)
            pool.wait_ge(head_mask_ready, 1)
            pool.wait_ge(v_pad_zero, 1)

            def rstd(s, lag, mv, ve, dst, mv_ready, ve_ready, ready):
                r = (s.u + lag) % 4
                s.wait(mv_ready, lag)
                nc.gpsimd.tensor_tensor(ve[:, r:r + 1], mv[:, r, 1:2], eps_sb[:, :], ALU.add).then_inc(ve_ready, 1)
                s.wait(ve_ready, lag)
                nc.gpsimd.tensor_tensor(dst[:, r:r + 1], ve[:, r:r + 1], minus_half[:, :], ALU.pow).then_inc(ready, 1)

            def slot(s):
                u = s.u
                if s.has(-1):
                    r = (u - 1) % 2
                    s.wait(recip_ready, -1)
                    s.wait(v_ready, -1)
                    s.wait(a_mm, -3)
                    for par in range(2):
                        src = v_sb[:, r, :].rearrange("p (g q d) -> p g q d", q=2, d=D)[:, :, par, :]
                        rec = recip[:, r, :].rearrange("p (g q a) -> p g q a", q=2, a=1)[:, :, par, :]
                        last = nc.gpsimd.tensor_tensor(v_pad[:, r, :, par, par * D:(par + 1) * D], src,
                                                       rec.to_broadcast([P, H // 2, D]), ALU.mult)
                    last.then_inc(v_pad_ready, 1)
                if s.has(-2):
                    s.wait(y_ready, -2)
                    if (u - 2) % 4 == 0 and s.has(-18):
                        s.wait_dma(stored, -18, 4)
                    nc.gpsimd.tensor_tensor(s_sb[:, (u - 2) % 16, :], x1_sb[:, (u - 2) % 4, :], y_sb[:, (u - 2) % 16, :],
                                            ALU.add).then_inc(s_ready, 1)
                if s.has(4):
                    if u % 2 == 0:
                        s.wait_dma(x_in, 4, 2)
                    s.wait(x1_ready, -4)
                    nc.gpsimd.tensor_tensor(xb_sb[:, (u + 4) % 8, :], x_sb[:, (u + 4) % 8, :], bo_sb[:, :], ALU.add).then_inc(xb_ready, 1)
                if u % 2 == 0 and s.has(2):
                    s.wait(q_raw_ready, 3)
                    s.wait(s_mm[J - 1], -1)
                    for par in range(2):
                        last = nc.gpsimd.tensor_tensor(q_eo[:, ((u + 2) // 2) % 2, :, :, par, :], q_raw[:, :, :, :],
                                                       head_mask[:, par:par + 1].rearrange("p (a b c) -> p a b c", a=1, b=1).to_broadcast([P, C, 2, T]),
                                                       ALU.mult)
                    last.then_inc(q_eo_ready, 2)
                if s.has(6):
                    rstd(s, 6, mv1, ve1, rstd1, mv1_ready, ve1_ready, rstd1_ready)
                for phase, lag, last_gelu in ((4, 12, 9), (5, 11, 10), (6, 10, 7), (7, 9, 8)):
                    if u % GROUP == phase and s.has(-lag, 2):
                        s.wait(gelu_ready, -last_gelu)
                        for b in range(2):
                            k = (u - lag + b) % 16
                            nc.gpsimd.tensor_tensor(z_sb[:, k, 0:E], z_sb[:, k, 0:E], y_sb[:, k, :], ALU.subtract).then_inc(d_ready, 1)
                if s.has(-1):
                    rstd(s, -1, mv2, ve2, rstd2, mv2_ready, ve2_ready, rstd2_ready)

            run(pool, slot, FIRST, LAST)


_INS = ["x", "ctx_1024", "L0_xattn_Wq", "L0_xattn_bq", "L0_xattn_Wkv", "L0_xattn_bkv", "L0_xattn_Wo", "L0_xattn_bo",
        "L0_ffn_w_router", "L0_ffn_w_block"]


def kernel(**inputs):
    import numpy as _np
    import concourse.bacc as _bacc
    from concourse import mybir as _mybir
    from concourse.bass_utils import run_bass_kernel_spmd as _run

    nc = _bacc.Bacc("TRN2", target_bir_lowering=False, num_devices=1)
    arrays, args = {}, []
    for name in _INS:
        a = _np.ascontiguousarray(inputs[name])
        arrays[f"in_{name}"] = a
        args.append(nc.dram_tensor(f"in_{name}", a.shape, _mybir.dt.from_np(a.dtype), kind="ExternalInput").ap())
    shape = inputs["x"].shape
    args.append(nc.dram_tensor("out", shape, _mybir.dt.float32, kind="ExternalOutput").ap())
    cross_attention_routed_ffn(nc, *args)
    r = _run(nc, [arrays], core_ids=[0])
    return r.results[0]["out"]
```

```python
from contextlib import ExitStack

import concourse.bass as bass
from concourse import mybir


def cross_attention_routed_ffn(
    nc: bass.Bass,
    x: bass.AP,
    ctx_in: bass.AP,
    w_q: bass.AP,
    b_q: bass.AP,
    w_kv: bass.AP,
    b_kv: bass.AP,
    w_o: bass.AP,
    b_o: bass.AP,
    w_router: bass.AP,
    w_block: bass.AP,
    out: bass.AP,
):
    f32 = mybir.dt.float32
    f32r = mybir.dt.float32r
    ALU = mybir.AluOpType
    ACT = mybir.ActivationFunctionType
    AX = mybir.AxisListType

    B, T, E = x.shape
    H = 16
    D = E // H
    P = 128
    C = E // P
    J = 4
    KEEP = int(T * 0.75)
    DROP = T - KEEP
    EPS = 1e-5
    LOWEST = -3.4028234663852886e38
    SCALE = 1.0 / D ** 0.5
    assert T == P and E == C * P and B % 16 == 0 and DROP % 8 == 0

    BODY = 16
    GROUP = 8
    DVE_SUMS = 1
    ZW = E + 2

    ctx = ExitStack()
    with ctx:
        def sb(name, shape, dt=f32):
            return ctx.enter_context(nc.sbuf_tensor(name, shape, dt))

        def sem(name):
            return ctx.enter_context(nc.semaphore(name))

        x_sb = sb("x_sb", [P, 8, E])
        c_sb = sb("c_sb", [P, 8, E])
        xb_sb = sb("xb_sb", [P, 8, E])
        xhat = sb("xhat", [P, 2, E])
        t_hi = sb("t_hi", [P, 4, 2, C, 2 * T], f32r)
        t_lo = sb("t_lo", [P, 4, 2, C, 2 * T], f32r)
        q_raw = sb("q_raw", [P, C, 2, T])
        q_eo = sb("q_eo", [P, 2, C, 2, 2, T])
        k_sb = sb("k_sb", [P, 2, C, 2 * T])
        v_sb = sb("v_sb", [P, 2, E])
        v_pad = sb("v_pad", [P, 2, H // 2, 2, 2 * D])
        e_sb = sb("e_sb", [P, 2, J, C, 2, T])
        o_hi = sb("o_hi", [P, 2, E], f32r)
        o_lo = sb("o_lo", [P, 2, E], f32r)
        x1_sb = sb("x1_sb", [P, 4, E])
        y_sb = sb("y_sb", [P, 16, E])
        y_hi = sb("y_hi", [P, 2, E], f32r)
        y_lo = sb("y_lo", [P, 2, E], f32r)
        z_sb = sb("z_sb", [P, 16, ZW])
        s_sb = sb("s_sb", [P, 16, E])
        w_hi = {n: sb(f"w_{n}_hi", [P, C, ZW if n == "z" else E], f32r) for n in "qkvoz"}
        w_lo = {n: sb(f"w_{n}_lo", [P, C, ZW if n == "z" else E], f32r) for n in "qkvoz"}
        bq_sb = sb("bq_sb", [P, C])
        bk_sb = sb("bk_sb", [P, C])
        bv_sb = sb("bv_sb", [P, E])
        bo_sb = sb("bo_sb", [P, E])
        ident = sb("ident", [P, P])
        head_mask = sb("head_mask", [P, 2])
        eps_sb = sb("eps_sb", [P, 1])
        minus_half = sb("minus_half", [P, 1])
        st1 = sb("st1", [P, 2, 6])
        mv1 = sb("mv1", [P, 4, 2])
        ve1 = sb("ve1", [P, 4])
        rstd1 = sb("rstd1", [P, 4])
        st2 = sb("st2", [P, 2, 6])
        mv2 = sb("mv2", [P, 4, 2])
        ve2 = sb("ve2", [P, 4])
        rstd2 = sb("rstd2", [P, 4])
        neg_max = sb("neg_max", [P, 2, H])
        sums = sb("sums", [P, 2, H])
        recip = sb("recip", [P, 2, H])
        fence_sb = sb("fence_sb", [1, 3])
        cand = sb("cand", [GROUP, T])
        top8 = sb("top8", [GROUP, 8])
        keep_row = sb("keep_row", [GROUP, T])
        keep_col = sb("keep_col", [P, 2, GROUP])

        raw = z_sb[:, :, :].rearrange("p b e -> p (b e)")
        raw_w, at = {}, 0
        for n in "qkvoz":
            width = ZW if n == "z" else E
            raw_w[n] = raw[:, at:at + C * width].rearrange("p (c e) -> p c e", c=C)
            at += C * width

        ps_s = ctx.enter_context(nc.psum_tensor("ps_s", [P, J, C, 2, T], f32))
        ps_a = ctx.enter_context(nc.psum_tensor("ps_a", [P, 512], f32))
        ps_y = ctx.enter_context(nc.psum_tensor("ps_y", [P, 512], f32))
        ps_attn, ps_proj = ps_a[:, 0:E], ps_a[:, E:2 * E]
        ps_vy = ps_y[:, 0:E]
        ps_cand, ps_keep = ps_y[0:GROUP, E:E + T], ps_y[:, E + T:E + T + GROUP]
        ps_t = ctx.enter_context(nc.psum_tensor("ps_t", [P, 512], f32))
        ps_q = ctx.enter_context(nc.psum_tensor("ps_q", [P, 512], f32))

        x_in = [sem(f"x_in{i}") for i in range(8)]
        c_in = [sem(f"c_in{i}") for i in range(8)]
        stored = [sem(f"stored{i}") for i in range(4)]
        w_in = {n: sem(f"w_{n}_in") for n in "qkvoz"}
        b_in = sem("b_in")
        const_ready = sem("const_ready")
        mask_step = sem("mask_step")
        v_pad_zero = sem("v_pad_zero")
        parity_ready = sem("parity_ready")
        head_mask_ready = sem("head_mask_ready")
        w_hi_ready = {n: sem(f"w_{n}_hi_ready") for n in "qkvoz"}
        w_lo_ready = {n: sem(f"w_{n}_lo_ready") for n in "qkvoz"}
        st1_ready, mv1_ready, ve1_ready, rstd1_ready = sem("st1_r"), sem("mv1_r"), sem("ve1_r"), sem("rstd1_r")
        st2_ready, mv2_ready, ve2_ready, rstd2_ready = sem("st2_r"), sem("mv2_r"), sem("ve2_r"), sem("rstd2_r")
        xhat_ready = sem("xhat_ready")
        xb_ready = sem("xb_ready")
        t_mm = sem("t_mm")
        t_hi_ready = sem("t_hi_ready")
        t_lo_ready = sem("t_lo_ready")
        q_mm = sem("q_mm")
        q_raw_ready = sem("q_raw_ready")
        q_eo_ready = sem("q_eo_ready")
        k_mm = sem("k_mm")
        k_ready = sem("k_ready")
        s_mm = [sem(f"s_mm{j}") for j in range(J)]
        max_ready = [sem(f"max_ready{j}") for j in range(J)]
        exp_ready = [sem(f"exp_ready{j}") for j in range(J)]
        sum_ready = sem("sum_ready")
        recip_ready = sem("recip_ready")
        v_mm = sem("v_mm")
        v_ready = sem("v_ready")
        v_pad_ready = sem("v_pad_ready")
        a_mm = sem("a_mm")
        o_hi_ready = sem("o_hi_ready")
        o_lo_ready = sem("o_lo_ready")
        o_mm = sem("o_mm")
        x1_ready = sem("x1_ready")
        y_ready = sem("y_ready")
        y_mm = sem("y_mm")
        y_hi_ready = sem("y_hi_ready")
        y_lo_ready = sem("y_lo_ready")
        z_mm = sem("z_mm")
        z_ready = sem("z_ready")
        s_ready = sem("s_ready")
        gelu_ready = sem("gelu_ready")
        d_ready = sem("d_ready")
        score_mm = sem("score_mm")
        cand_ready = sem("cand_ready")
        top_found = sem("top_found")
        top_dropped = sem("top_dropped")
        keep_row_ready = sem("keep_row_ready")
        keep_mm = sem("keep_mm")
        keep_col_ready = sem("keep_col_ready")
        final_ready = sem("final_ready")

        block = ctx.enter_context(nc.Block())

        class Slot:

            def __init__(self, eng, i, u, values):
                self.eng, self.i, self.u, self.values = eng, i, u, values

            def has(self, lag, count=1):
                if not isinstance(self.i, int):
                    return True
                b = BODY * self.i + self.u + lag
                return 0 <= b and b + count <= B

            def at(self, n):
                return isinstance(self.i, int) and BODY * self.i + self.u == n

            def after(self, n):
                return isinstance(self.i, int) and BODY * self.i + self.u > n

            def rows(self, dram, lag, count):
                b = self.u + lag
                view = dram.rearrange("(n b) t e -> n t b e", b=BODY)
                return view[self.i + b // BODY, :, b % BODY:b % BODY + count, :]

            def value(self, k):
                if isinstance(self.i, int):
                    assert BODY * self.i + k > 0
                    return min(BODY * self.i + k, B)
                assert BODY + k > 0
                if k not in self.values:
                    self.values[k] = self.eng.snap(self.i * BODY + k)
                return self.values[k]

            def upto(self, lag):
                return self.value(self.u + lag + 1)

            def dma(self, lag, per):
                return (self.u + lag) % 16 // per

            def landed(self, lag):
                return self.value((self.u + lag) // 16 * 16 + 16)

        def run(eng, slot, first, last):
            n = B // BODY
            for u in range(first, BODY):
                slot(Slot(eng, 0, u, {}))
            with eng.Fori(1, n - 1) as i:
                values = {}
                for u in range(BODY):
                    slot(Slot(eng, i, u, values))
            for u in range(last - (n - 1) * BODY):
                slot(Slot(eng, n - 1, u, {}))

        def group_at(s, phase, lag):
            return s.u % GROUP == phase and s.has(-lag, GROUP)

        WEIGHTS = (("q", -4), ("k", -3), ("v", -2), ("o", -1), ("z", -1))

        FIRST, LAST = -6, B + 10

        @block.sync
        def _(sp):
            def load(s):
                if s.u % 2 == 0 and s.has(10):
                    if s.has(3):
                        sp.wait_ge(xhat_ready, s.upto(3))
                        sp.wait_ge(xb_ready, s.upto(3))
                        sp.wait_ge(t_mm, s.upto(3))
                    r = (s.u + 10) % 8
                    n = ((s.u + 10) // 2) % 8
                    sp.dma_start(x_sb[:, r:r + 2, :], s.rows(x, 10, 2)).then_inc(x_in[n], 16)
                    sp.dma_start(c_sb[:, r:r + 2, :], s.rows(ctx_in, 10, 2)).then_inc(c_in[n], 16)

            for u in (-10, -8):
                load(Slot(sp, 0, u, {}))
            for n, src in (("q", w_q), ("k", w_kv[:, 0:E])):
                sp.dma_start(raw_w[n], src.rearrange("(c p) e -> p c e", p=P)).then_inc(w_in[n], 16)
            with nc.allow_non_contiguous_dma(reason="vectors of 256 elements, once"):
                sp.dma_start(bq_sb[:, :], b_q.rearrange("(c p) -> p c", p=P)).then_inc(b_in, 16)
                sp.dma_start(bk_sb[:, :], b_kv[0:E].rearrange("(c p) -> p c", p=P)).then_inc(b_in, 16)
            sp.dma_start(bv_sb[:, :], b_kv[E:2 * E].rearrange("(a e) -> a e", a=1).to_broadcast([P, E])).then_inc(b_in, 16)
            sp.dma_start(bo_sb[:, :], b_o.rearrange("(a e) -> a e", a=1).to_broadcast([P, E])).then_inc(b_in, 16)
            load(Slot(sp, 0, -6, {}))
            for n, src in (("v", w_kv[:, E:2 * E]), ("o", w_o)):
                sp.dma_start(raw_w[n], src.rearrange("(c p) e -> p c e", p=P)).then_inc(w_in[n], 16)
            sp.dma_start(raw_w["z"][:, :, 0:E], w_block.rearrange("(c p) e -> p c e", p=P)).then_inc(w_in["z"], 16)
            with nc.allow_non_contiguous_dma(reason="a vector of 256 elements, once"):
                sp.dma_start(raw_w["z"][:, :, E:E + 1], w_router.rearrange("(c p a) -> p c a", p=P, a=1)).then_inc(w_in["z"], 16)

            def slot(s):
                load(s)
                for phase, lag in ((0, 16), (2, 14)):
                    if s.u % GROUP == phase and s.has(-lag, 4):
                        sp.wait_ge(final_ready, s.upto(3 - lag))
                        r = (s.u - lag) % 16
                        sp.dma_start(s.rows(out, -lag, 4),
                                     s_sb[:, r:r + 4, :]).then_inc(stored[(r // 4) % 4], 16)

            run(sp, slot, -4, LAST + 3)
            for n in range(4):
                sp.wait_ge(stored[n], B)

        @block.tensor
        def _(pe):
            pe.wait_ge(const_ready, 1)

            def three_terms(dst, lhs, rhs):
                terms = [(a, b) for a, b in ((0, 0), (1, 0), (0, 1))]
                for c in range(C):
                    for n, (a, b) in enumerate(terms):
                        last = nc.tensor.matmul(dst, lhs(a, c), rhs(b, c), start=(c == 0 and n == 0),
                                                stop=(c == C - 1 and n == len(terms) - 1))
                return last

            def scores(s, j):
                if not s.has(0):
                    return
                r2, h = (s.u // 2) % 2, s.u % 2
                if j == 0 and h == 0:
                    pe.wait_ge(q_eo_ready, s.upto(1))
                    pe.wait_ge(k_ready, s.upto(1))
                if s.has(-1):
                    pe.wait_ge(exp_ready[j], s.upto(-1))
                rows = slice(32 * j, 32 * j + 32)
                for c in range(C):
                    mm = nc.tensor.matmul(ps_s[:, j, c, :, :], k_sb[rows, r2, c, h * T:(h + 1) * T],
                                          q_eo[rows, r2, c, h, :, :], start=True, stop=True)
                mm.then_inc(s_mm[j], 1)

            def transpose_inputs(s):
                if not s.has(4):
                    return
                pe.wait_ge(xhat_ready, s.upto(4))
                if s.u % 2 == 0:
                    pe.wait_ge(c_in[s.dma(4, 2)], s.landed(4))
                if s.has(3):
                    pe.wait_ge(t_lo_ready, s.upto(3))
                if s.has(-4):
                    pe.wait_ge(z_ready, s.upto(-4))
                for kind in range(2):
                    for c in range(C):
                        src = (xhat[:, s.u % 2, c * P:(c + 1) * P] if kind == 0
                               else c_sb[:, (s.u + 4) % 8, c * P:(c + 1) * P])
                        n = kind * C + c
                        mm = nc.tensor.transpose(ps_t[:, n * T:(n + 1) * T], src, ident[:, :])
                mm.then_inc(t_mm, 1)

            def values(s):
                if not s.has(0):
                    return
                if s.has(-3):
                    pe.wait_ge(y_lo_ready, s.upto(-3))
                if group_at(s, 3, 11):
                    pe.wait_ge(cand_ready, s.upto(-4))
                if group_at(s, 6, 14):
                    pe.wait_ge(keep_col_ready, s.upto(-7))
                if s.at(0):
                    pe.wait_ge(w_lo_ready["v"], 1)
                pair, h = (s.u // 2) % 4, s.u % 2
                three_terms(ps_vy,
                            lambda a, c: (t_hi, t_lo)[a][:, pair, 1, c, h * T:(h + 1) * T],
                            lambda a, c: (w_hi, w_lo)[a]["v"][:, c, :]).then_inc(v_mm, 1)

            def block_product(s):
                if not s.has(-3):
                    return
                pe.wait_ge(y_lo_ready, s.upto(-3))
                pe.wait_ge(t_lo_ready, s.upto(4))
                if s.at(3):
                    pe.wait_ge(w_lo_ready["z"], 1)
                three_terms(ps_t[:, 0:ZW],
                            lambda a, c: (y_hi, y_lo)[a][:, (s.u - 3) % 2, c * T:(c + 1) * T],
                            lambda a, c: (w_hi, w_lo)[a]["z"][:, c, :]).then_inc(z_mm, 1)

            def attention(s):
                if not s.has(-1):
                    return
                r = (s.u - 1) % 2
                pe.wait_ge(v_pad_ready, s.upto(-1))
                if s.has(-2):
                    pe.wait_ge(x1_ready, s.upto(-2))
                for c in range(C):
                    for par in range(2):
                        for j in range(J):
                            mm = nc.tensor.matmul(ps_attn[32 * j:32 * j + 32, c * T:(c + 1) * T],
                                                  v_pad[:, r, c * J + j, par, :], e_sb[:, r, j, c, par, :],
                                                  start=(par == 0), stop=(par == 1))
                mm.then_inc(a_mm, 1)

            def queries_or_keys(s):
                kind, lag = (0, 3) if s.u % 2 == 1 else (1, 2)
                if not s.has(lag):
                    return
                pair = ((s.u + lag) // 2) % 4
                if kind == 0:
                    pe.wait_ge(t_lo_ready, s.upto(4))
                    if s.has(2):
                        pe.wait_ge(k_ready, s.upto(2))
                else:
                    pe.wait_ge(q_raw_ready, s.upto(3))
                w = "qk"[kind]
                if s.at(-3) or s.at(-2):
                    pe.wait_ge(w_lo_ready[w], 1)
                for m in range(C):
                    mm = three_terms(ps_q[:, m * 2 * T:(m + 1) * 2 * T],
                                     lambda a, c: (w_hi, w_lo)[a][w][:, c, m * P:(m + 1) * P],
                                     lambda a, c: (t_hi, t_lo)[a][:, pair, kind, c, :])
                mm.then_inc((q_mm, k_mm)[kind], 2)

            def projection(s):
                if not s.has(-1):
                    return
                pe.wait_ge(o_lo_ready, s.upto(-1))
                if s.at(1):
                    pe.wait_ge(w_lo_ready["o"], 1)
                three_terms(ps_proj,
                            lambda a, c: (o_hi, o_lo)[a][:, (s.u - 1) % 2, c * T:(c + 1) * T],
                            lambda a, c: (w_hi, w_lo)[a]["o"][:, c, :]).then_inc(o_mm, 1)

            def transpose_y(s):
                if not s.has(-2):
                    return
                pe.wait_ge(y_ready, s.upto(-2))
                pe.wait_ge(v_ready, s.upto(0))
                for c in range(C):
                    mm = nc.tensor.transpose(ps_vy[:, c * T:(c + 1) * T], y_sb[:, (s.u - 2) % 16, c * P:(c + 1) * P], ident[:, :])
                mm.then_inc(y_mm, 1)

            def router(s):
                if group_at(s, 2, 10):
                    pe.wait_ge(z_ready, s.upto(-3))
                    pe.wait_ge(v_ready, s.upto(0))
                    r = (s.u - 10) % 16
                    nc.tensor.transpose(ps_cand, z_sb[:, r:r + GROUP, E], ident[:, :]).then_inc(score_mm, 8)
                if group_at(s, 5, 13):
                    pe.wait_ge(keep_row_ready, s.upto(-6))
                    pe.wait_ge(v_ready, s.upto(0))
                    nc.tensor.transpose(ps_keep, keep_row[:, :], ident[0:GROUP, 0:GROUP]).then_inc(keep_mm, 8)

            def slot(s):
                scores(s, 0)
                transpose_inputs(s)
                scores(s, 1)
                scores(s, 2)
                attention(s)
                scores(s, 3)
                values(s)
                block_product(s)
                queries_or_keys(s)
                projection(s)
                router(s)
                transpose_y(s)

            run(pe, slot, FIRST, LAST)

        @block.scalar
        def _(act):
            def weights_high(s):
                for n, first in WEIGHTS:
                    if s.at(first):
                        act.wait_ge(w_in[n], 32 if n == "z" else 16)
                        if n == "z":
                            act.wait_ge(const_ready, 1)
                        nc.scalar.copy(w_hi[n][:, :, :], raw_w[n]).then_inc(w_hi_ready[n], 1)

            def exps(s, j):
                if not s.has(0):
                    return
                r = s.u % 2
                act.wait_ge(max_ready[j], s.upto(0))
                if j == 0 and s.has(-2):
                    act.wait_ge(a_mm, s.upto(-2))
                    act.wait_ge(recip_ready, s.upto(-2))
                for c in range(C):
                    for par in range(2):
                        h = c * 2 * J + 2 * j + par
                        extra = {} if j == DVE_SUMS else {"accum_out": sums[:, r, h:h + 1]}
                        last = nc.scalar.activation(e_sb[:, r, j, c, par, :], ps_s[:, j, c, par, :], ACT.Exp,
                                                    bias=neg_max[:, r, h:h + 1], **extra)
                last.then_inc(exp_ready[j], 1)

            def y_high(s):
                if s.has(-3):
                    act.wait_ge(y_mm, s.upto(-3))
                    if s.has(-5):
                        act.wait_ge(z_mm, s.upto(-5))
                    nc.scalar.copy(y_hi[:, (s.u - 3) % 2, :], ps_vy).then_inc(y_hi_ready, 1)

            def inputs_high(s):
                if s.has(4):
                    act.wait_ge(t_mm, s.upto(4))
                    if s.has(-4):
                        act.wait_ge(v_mm, s.upto(-4))
                    pair, h = ((s.u + 4) // 2) % 4, s.u % 2
                    nc.scalar.copy(t_hi[:, pair, :, :, h * T:(h + 1) * T].rearrange("p k c t -> p (k c) t"),
                                   ps_t[:, :].rearrange("p (n t) -> p n t", t=T)).then_inc(t_hi_ready, 1)

            def keys(s):
                if s.u % 2 == 1 and s.has(1):
                    act.wait_ge(k_mm, s.upto(2))
                    if s.has(-2):
                        act.wait_ge(s_mm[J - 1], s.upto(-2))
                    if s.at(-1):
                        act.wait_ge(b_in, 64)
                    for c in range(C):
                        last = nc.scalar.activation(k_sb[:, ((s.u + 1) // 2) % 2, c, :], ps_q[:, c * 2 * T:(c + 1) * 2 * T],
                                                    ACT.Identity, bias=bk_sb[:, c:c + 1])
                    last.then_inc(k_ready, 2)

            def attention_high(s):
                if s.has(-1):
                    act.wait_ge(a_mm, s.upto(-1))
                    if s.has(-3):
                        act.wait_ge(o_mm, s.upto(-3))
                    nc.scalar.copy(o_hi[:, (s.u - 1) % 2, :], ps_attn).then_inc(o_hi_ready, 1)

            def product_copy(s):
                if s.has(-3):
                    act.wait_ge(z_mm, s.upto(-3))
                    if s.has(-16):
                        act.wait_ge(final_ready, s.upto(-16))
                    if s.at(3):
                        act.wait_ge(w_lo_ready["z"], 1)
                    nc.scalar.copy(z_sb[:, (s.u - 3) % 16, :], ps_t[:, 0:ZW]).then_inc(z_ready, 1)

            def gelu(s, first, count):
                act.wait_ge(z_ready, s.upto(first + count - 1))
                r = (s.u + first) % 16
                z = z_sb[:, r:r + count, 0:E]
                nc.scalar.activation(z, z, ACT.Gelu_apprx_tanh).then_inc(gelu_ready, count)

            def slot(s):
                weights_high(s)
                keys(s)
                y_high(s)
                if s.at(B):
                    gelu(s, -GROUP, 5)
                inputs_high(s)
                exps(s, 0)
                if s.u % GROUP != 3:
                    attention_high(s)
                    exps(s, 1)
                    exps(s, 2)
                    product_copy(s)
                    exps(s, 3)
                else:
                    exps(s, 1)
                    attention_high(s)
                    exps(s, 2)
                    exps(s, 3)
                    product_copy(s)
                    if s.has(-11, GROUP) and not s.at(B + 3):
                        gelu(s, -11, GROUP)
                if s.at(B) or s.at(B + 1) or s.at(B + 2):
                    gelu(s, -3, 1)

            run(act, slot, FIRST, LAST)

        @block.vector
        def _(dve):
            nc.vector.memset(v_pad[:, :, :, :, :], 0.0).then_inc(v_pad_zero, 1)
            dve.wait_ge(const_ready, 1)
            nc.vector.tensor_reduce(head_mask[:, :], ident[:, :].rearrange("p (g q d) -> p q g d", q=2, d=D), AX.XY,
                                    ALU.add).then_inc(parity_ready, 1)
            dve.wait_ge(parity_ready, 1)
            nc.vector.tensor_scalar(head_mask[:, :], head_mask[:, :], SCALE, None, ALU.mult).then_inc(head_mask_ready, 1)
            def weights_low(s):
                for n, first in WEIGHTS:
                    if s.at(first):
                        dve.wait_ge(w_hi_ready[n], 1)
                        nc.vector.tensor_tensor(w_lo[n][:, :, :], raw_w[n], w_hi[n][:, :, :].bitcast(f32),
                                                ALU.subtract).then_inc(w_lo_ready[n], 1)

            def maxima(s, j):
                if not s.has(0):
                    return
                dve.wait_ge(s_mm[j], s.upto(0))
                nc.vector.tensor_reduce(neg_max[:, s.u % 2, :].rearrange("p (c j q) -> p j c q", c=C, j=J)[:, j, :, :],
                                        ps_s[:, j, :, :, :], AX.X, ALU.max, negate=True).then_inc(max_ready[j], 1)

            def residual(s):
                if s.has(-2):
                    dve.wait_ge(o_mm, s.upto(-2))
                    dve.wait_ge(xb_ready, s.upto(-2))
                    if s.has(-6):
                        dve.wait_ge(s_ready, s.upto(-6))
                    nc.vector.tensor_tensor(x1_sb[:, (s.u - 2) % 4, :], ps_proj, xb_sb[:, (s.u - 2) % 8, :],
                                            ALU.add).then_inc(x1_ready, 1)

            def stats2(s):
                if s.has(-2):
                    dve.wait_ge(x1_ready, s.upto(-2))
                    nc.vector.bn_stats(st2[:, (s.u - 2) % 2, :], x1_sb[:, (s.u - 2) % 4, :]).then_inc(st2_ready, 1)

            def aggregate2(s):
                if s.has(-2):
                    dve.wait_ge(st2_ready, s.upto(-2))
                    fence(1)
                    nc.vector.bn_aggr(mv2[:, (s.u - 2) % 4, :], st2[:, (s.u - 2) % 2, :]).then_inc(mv2_ready, 1)

            def norm2(s):
                if s.has(-2):
                    r = (s.u - 2) % 4
                    dve.wait_ge(rstd2_ready, s.upto(-2))
                    if s.has(-16):
                        dve.wait_ge(d_ready, s.upto(-16))
                        dve.wait_ge(s_ready, s.upto(-16))
                    nc.vector.tensor_scalar(y_sb[:, (s.u - 2) % 16, :], x1_sb[:, r, :], mv2[:, r, 0:1], rstd2[:, r:r + 1],
                                            ALU.subtract, ALU.mult).then_inc(y_ready, 1)

            def stats1(s):
                if s.has(6):
                    if s.u % 2 == 0:
                        dve.wait_ge(x_in[s.dma(6, 2)], s.landed(6))
                    nc.vector.bn_stats(st1[:, s.u % 2, :], x_sb[:, (s.u + 6) % 8, :]).then_inc(st1_ready, 1)

            def aggregate1(s):
                if s.has(6):
                    dve.wait_ge(st1_ready, s.upto(6))
                    fence(0)
                    nc.vector.bn_aggr(mv1[:, (s.u + 6) % 4, :], st1[:, s.u % 2, :]).then_inc(mv1_ready, 1)

            def norm1(s):
                if s.has(5):
                    r = (s.u + 5) % 4
                    dve.wait_ge(rstd1_ready, s.upto(5))
                    if s.has(3):
                        dve.wait_ge(t_mm, s.upto(3))
                    nc.vector.tensor_scalar(xhat[:, (s.u + 5) % 2, :], x_sb[:, (s.u + 5) % 8, :], mv1[:, r, 0:1],
                                            rstd1[:, r:r + 1], ALU.subtract, ALU.mult).then_inc(xhat_ready, 1)

            def inverse_sums(s):
                if s.has(-1):
                    dve.wait_ge(exp_ready[J - 1], s.upto(-1))
                    dve.wait_ge(sum_ready, s.upto(-1))
                    if s.has(-3):
                        dve.wait_ge(v_pad_ready, s.upto(-3))
                    nc.vector.reciprocal(recip[:, (s.u - 1) % 2, :], sums[:, (s.u - 1) % 2, :]).then_inc(recip_ready, 1)

            def dve_sums(s):
                if s.has(0):
                    dve.wait_ge(exp_ready[DVE_SUMS], s.upto(0))
                    nc.vector.tensor_reduce(
                        sums[:, s.u % 2, :].rearrange("p (c j q) -> p j c q", c=C, j=J)[:, DVE_SUMS, :, :],
                        e_sb[:, s.u % 2, DVE_SUMS, :, :, :], AX.X, ALU.add).then_inc(sum_ready, 1)

            def inputs_low(s):
                if s.has(4):
                    pair, h = ((s.u + 4) // 2) % 4, s.u % 2
                    dve.wait_ge(t_hi_ready, s.upto(4))
                    part = (slice(None), pair, slice(None), slice(None), slice(h * T, (h + 1) * T))
                    nc.vector.tensor_tensor(t_lo[part].rearrange("p k c t -> p (k c) t"),
                                            ps_t[:, :].rearrange("p (n t) -> p n t", t=T),
                                            t_hi[part].rearrange("p k c t -> p (k c) t").bitcast(f32),
                                            ALU.subtract).then_inc(t_lo_ready, 1)

            def y_low(s):
                if s.has(-3):
                    dve.wait_ge(y_hi_ready, s.upto(-3))
                    nc.vector.tensor_tensor(y_lo[:, (s.u - 3) % 2, :], ps_vy, y_hi[:, (s.u - 3) % 2, :].bitcast(f32),
                                            ALU.subtract).then_inc(y_lo_ready, 1)

            def attention_low(s):
                if s.has(-1):
                    dve.wait_ge(o_hi_ready, s.upto(-1))
                    nc.vector.tensor_tensor(o_lo[:, (s.u - 1) % 2, :], ps_attn, o_hi[:, (s.u - 1) % 2, :].bitcast(f32),
                                            ALU.subtract).then_inc(o_lo_ready, 1)

            def queries(s):
                if s.u % 2 == 0 and s.has(2):
                    dve.wait_ge(q_mm, s.upto(3))
                    if s.has(1):
                        dve.wait_ge(q_eo_ready, s.upto(1))
                    if s.at(-2):
                        dve.wait_ge(b_in, 64)
                    nc.vector.tensor_tensor(q_raw[:, :, :, :].rearrange("p c b t -> p c (b t)"),
                                            ps_q[:, :].rearrange("p (c t) -> p c t", c=C),
                                            bq_sb[:, :].rearrange("p (c a) -> p c a", a=1).to_broadcast([P, C, 2 * T]),
                                            ALU.add).then_inc(q_raw_ready, 2)

            def values(s):
                if s.has(0):
                    dve.wait_ge(v_mm, s.upto(0))
                    if s.has(-2):
                        dve.wait_ge(v_pad_ready, s.upto(-2))
                    nc.vector.tensor_tensor(v_sb[:, s.u % 2, :], ps_vy, bv_sb[:, :], ALU.add).then_inc(v_ready, 1)

            def fence(n):
                nc.vector.memset(fence_sb[:, n:n + 1], 0.0)

            def router(s, step):
                phase = (3, 3, 3, 3, 4, 4, 4, 4, 5, 5, 6)[step]
                lag = phase + GROUP
                if not group_at(s, phase, lag):
                    return
                if step == 0:
                    dve.wait_ge(score_mm, s.upto(7 - lag))
                    nc.vector.tensor_scalar(cand[:, :], ps_cand[:, ::-1], -1.0, None, ALU.mult).then_inc(cand_ready, 8)
                elif step <= 8:
                    rnd, replace = divmod(step - 1, 2)
                    if replace:
                        dve.wait_ge(top_found, s.upto(2 * rnd + 1 - lag))
                        fence(2)
                        nc.vector.match_replace(cand[:, :], top8[:, :], cand[:, :], LOWEST).then_inc(top_dropped, 2)
                    else:
                        if rnd == 0:
                            dve.wait_ge(cand_ready, s.upto(7 - lag))
                        else:
                            dve.wait_ge(top_dropped, s.upto(2 * rnd - 1 - lag))
                        fence(2)
                        nc.vector.max(top8[:, :], cand[:, :]).then_inc(top_found, 2)
                elif step == 9:
                    dve.wait_ge(top_dropped, s.upto(7 - lag))
                    if s.has(-1 - lag):
                        dve.wait_ge(keep_mm, s.upto(-1 - lag))
                    nc.vector.tensor_scalar(keep_row[:, ::-1], cand[:, :], LOWEST, None, ALU.is_gt).then_inc(keep_row_ready, 8)
                elif step == 10:
                    dve.wait_ge(keep_mm, s.upto(7 - lag))
                    nc.vector.tensor_copy(keep_col[:, ((s.u - lag) // 8) % 2, :], ps_keep).then_inc(keep_col_ready, 8)

            def final(s):
                for phase, lag in ((6, 14), (7, 13), (0, 12), (1, 11)):
                    if s.u % GROUP == phase and s.has(-lag, 2):
                        dve.wait_ge(d_ready, s.upto(1 - lag))
                        if phase == 6:
                            dve.wait_ge(keep_col_ready, s.upto(7 - lag))
                        for b in range(2):
                            k = s.u - lag + b
                            nc.vector.scalar_tensor_tensor(s_sb[:, k % 16, :], z_sb[:, k % 16, 0:E],
                                                           keep_col[:, (k // 8) % 2, k % 8:k % 8 + 1], s_sb[:, k % 16, :],
                                                           ALU.mult, ALU.add).then_inc(final_ready, 1)

            def slot(s):
                stats1(s)
                if not s.at(-4):
                    weights_low(s)
                queries(s)
                router(s, 4)
                inverse_sums(s)
                maxima(s, 0)
                residual(s)
                norm1(s)
                maxima(s, 1)
                router(s, 5)
                aggregate1(s)
                stats2(s)
                maxima(s, 2)
                router(s, 6)
                router(s, 8)
                y_low(s)
                router(s, 0)
                router(s, 10)
                router(s, 1)
                aggregate2(s)
                inputs_low(s)
                maxima(s, 3)
                if s.at(-4):
                    weights_low(s)
                router(s, 2)
                values(s)
                router(s, 9)
                norm2(s)
                attention_low(s)
                router(s, 3)
                final(s)
                dve_sums(s)
                router(s, 7)

            run(dve, slot, FIRST, LAST)

        @block.gpsimd
        def _(pool):
            nc.gpsimd.memset(ident[:, :], 0.0).then_inc(mask_step, 1)
            nc.gpsimd.memset(eps_sb[:, :], EPS).then_inc(mask_step, 1)
            nc.gpsimd.memset(minus_half[:, :], -0.5).then_inc(mask_step, 1)
            nc.gpsimd.memset(raw_w["z"][:, :, E + 1:E + 2], 0.0).then_inc(mask_step, 1)
            pool.wait_ge(mask_step, 4)
            nc.gpsimd.affine_select(out=ident[:, :], in_=ident[:, :], compare_op=ALU.not_equal, fill=1.0, base=0,
                                    pattern=[[-1, P]], channel_multiplier=1).then_inc(const_ready, 1)
            pool.wait_ge(head_mask_ready, 1)
            pool.wait_ge(v_pad_zero, 1)

            def rstd(s, lag, mv, ve, dst, mv_ready, ve_ready, ready):
                r = (s.u + lag) % 4
                pool.wait_ge(mv_ready, s.upto(lag))
                nc.gpsimd.tensor_tensor(ve[:, r:r + 1], mv[:, r, 1:2], eps_sb[:, :], ALU.add).then_inc(ve_ready, 1)
                pool.wait_ge(ve_ready, s.upto(lag))
                nc.gpsimd.tensor_tensor(dst[:, r:r + 1], ve[:, r:r + 1], minus_half[:, :], ALU.pow).then_inc(ready, 1)

            def values_over_sums(s):
                if s.has(-1):
                    r = (s.u - 1) % 2
                    pool.wait_ge(recip_ready, s.upto(-1))
                    pool.wait_ge(v_ready, s.upto(-1))
                    if s.has(-3):
                        pool.wait_ge(a_mm, s.upto(-3))
                    for par in range(2):
                        src = v_sb[:, r, :].rearrange("p (g q d) -> p g q d", q=2, d=D)[:, :, par, :]
                        rec = recip[:, r, :].rearrange("p (g q a) -> p g q a", q=2, a=1)[:, :, par, :]
                        last = nc.gpsimd.tensor_tensor(v_pad[:, r, :, par, par * D:(par + 1) * D], src,
                                                       rec.to_broadcast([P, H // 2, D]), ALU.mult)
                    last.then_inc(v_pad_ready, 1)

            def residual_sum(s):
                if s.has(-3):
                    pool.wait_ge(y_ready, s.upto(-3))
                    if (s.u - 3) % 4 == 0 and s.has(-19):
                        pool.wait_ge(stored[s.dma(-19, 4)], s.landed(-19))
                    nc.gpsimd.tensor_tensor(s_sb[:, (s.u - 3) % 16, :], x1_sb[:, (s.u - 3) % 4, :], y_sb[:, (s.u - 3) % 16, :],
                                            ALU.add).then_inc(s_ready, 1)

            def queries_even_odd(s):
                if s.u % 2 == 0 and s.has(2):
                    pool.wait_ge(q_raw_ready, s.upto(3))
                    if s.has(-1):
                        pool.wait_ge(s_mm[J - 1], s.upto(-1))
                    for par in range(2):
                        last = nc.gpsimd.tensor_tensor(q_eo[:, ((s.u + 2) // 2) % 2, :, :, par, :], q_raw[:, :, :, :],
                                                       head_mask[:, par:par + 1].rearrange("p (a b c) -> p a b c", a=1, b=1).to_broadcast([P, C, 2, T]),
                                                       ALU.mult)
                    last.then_inc(q_eo_ready, 2)

            def input_and_bias(s):
                if s.has(3):
                    if s.u % 2 == 1:
                        pool.wait_ge(x_in[s.dma(3, 2)], s.landed(3))
                    if s.has(-5):
                        pool.wait_ge(x1_ready, s.upto(-5))
                    if s.at(-3):
                        pool.wait_ge(b_in, 64)
                    nc.gpsimd.tensor_tensor(xb_sb[:, (s.u + 3) % 8, :], x_sb[:, (s.u + 3) % 8, :], bo_sb[:, :],
                                            ALU.add).then_inc(xb_ready, 1)

            def gelu_minus_y(s, first, count, known):
                if not s.has(first, count):
                    return
                pool.wait_ge(gelu_ready, s.upto(known))
                for b in range(count):
                    k = (s.u + first + b) % 16
                    nc.gpsimd.tensor_tensor(z_sb[:, k, 0:E], z_sb[:, k, 0:E], y_sb[:, k, :], ALU.subtract).then_inc(d_ready, 1)

            def slot(s):
                residual_sum(s)
                values_over_sums(s)
                input_and_bias(s)
                queries_even_odd(s)
                if s.has(-2):
                    rstd(s, -2, mv2, ve2, rstd2, mv2_ready, ve2_ready, rstd2_ready)
                phase = s.u % GROUP
                if phase >= 4 and not s.after(B):
                    gelu_minus_y(s, phase - 16, 2, -phase - 1)
                if s.at(B + 1):
                    gelu_minus_y(s, -9, 3, -7)
                if s.at(B + 2):
                    gelu_minus_y(s, -7, 3, -5)
                if s.at(B + 3):
                    gelu_minus_y(s, -5, 2, -4)
                if s.has(6):
                    rstd(s, 6, mv1, ve1, rstd1, mv1_ready, ve1_ready, rstd1_ready)

            run(pool, slot, FIRST, LAST)


_INS = ["x", "ctx_1024", "L0_xattn_Wq", "L0_xattn_bq", "L0_xattn_Wkv", "L0_xattn_bkv", "L0_xattn_Wo", "L0_xattn_bo",
        "L0_ffn_w_router", "L0_ffn_w_block"]


def kernel(**inputs):
    import numpy as _np
    import concourse.bacc as _bacc
    from concourse import mybir as _mybir
    from concourse.bass_utils import run_bass_kernel_spmd as _run

    nc = _bacc.Bacc("TRN2", target_bir_lowering=False, num_devices=1)
    arrays, args = {}, []
    for name in _INS:
        a = _np.ascontiguousarray(inputs[name])
        arrays[f"in_{name}"] = a
        args.append(nc.dram_tensor(f"in_{name}", a.shape, _mybir.dt.from_np(a.dtype), kind="ExternalInput").ap())
    shape = inputs["x"].shape
    args.append(nc.dram_tensor("out", shape, _mybir.dt.float32, kind="ExternalOutput").ap())
    cross_attention_routed_ffn(nc, *args)
    r = _run(nc, [arrays], core_ids=[0])
    return r.results[0]["out"]
```
